# Optimizing a Trainium2 kernel written in Bass

```python
import numpy as np
import jax
import jax.numpy as jnp

def _softmax(x, axis=-1):
    return jax.nn.softmax(x, axis=axis)

def _gelu(x):
    return jax.nn.gelu(x, approximate=True)

def _silu(x):
    return jax.nn.silu(x)

def _sigmoid(x):
    return jax.nn.sigmoid(x)

def _layernorm(x, axis=-1, eps=1e-05):
    m = jnp.mean(x, axis=axis, keepdims=True)
    v = jnp.var(x, axis=axis, keepdims=True)
    return (x - m) / jnp.sqrt(v + eps)

def _scatter_add(tgt, idx, src, axis=0):
    return tgt.at[idx].add(src)

def _segment_sum(src, seg, n):
    return jax.ops.segment_sum(src, seg, n)
kernel_name = 'mk_adj_preln_d2_adj_r2_2010b6'

def setup_inputs(seed: int=0):
    np.random.seed(seed)
    _w = jnp.asarray

    def _rec_inputs():
        import jax
        import jax.numpy as jnp
        _gk = jax.random.key(seed)
        x = -0.000929 + 1 * jax.random.normal(jax.random.fold_in(_gk, 1), (8192, 64), jnp.float32)
        _a = jax.random.bernoulli(jax.random.fold_in(_gk, 2), 0.000244141, (8192, 8192))
        _a = jnp.logical_or(_a, jnp.swapaxes(_a, -1, -2))
        _a = jnp.logical_or(_a, jnp.eye(8192, dtype=bool))
        _af = _a.astype(jnp.float32)
        _af = _af * jax.random.uniform(jax.random.fold_in(_gk, 3), (8192, 8192), jnp.float32, 0.05, 1)
        adj = _af
        return (x, adj)
    x, adj = _rec_inputs()

    def _L0_gnn_setup():
        import jax, jax.numpy as jnp
        import numpy as np
        P_DROP = 0.1
        key = jax.random.key(seed)
        k1, k2, k3 = jax.random.split(key, 3)
        N, D = (8192, 64)
        x = jax.random.normal(k1, (N, D), dtype=jnp.float32)
        adj = jax.random.uniform(k2, (N, N), dtype=jnp.float32)
        u = jax.random.uniform(k3, (N, D), dtype=jnp.float32)
        return {'x': x, 'adj': adj, 'u': u}
    _L0_gnn_all = _L0_gnn_setup()
    _L0_gnn_in = {k: v for k, v in _L0_gnn_all.items() if k in ('u',)}
    del _L0_gnn_all

    def _L1_gnn_setup():
        import jax, jax.numpy as jnp
        import numpy as np
        N = 8192
        F_IN = 64
        F_OUT = 64
        key = jax.random.key(seed)
        k1, k2, k3 = jax.random.split(key, 3)
        inp = jax.random.normal(k1, (N, F_IN), dtype=jnp.float32)
        adj = jax.random.uniform(k2, (N, N), dtype=jnp.float32)
        limit = np.sqrt(6.0 / (F_IN + F_OUT)).astype(np.float32)
        W = jax.random.uniform(k3, (F_IN, F_OUT), dtype=jnp.float32, minval=-limit, maxval=limit)
        b = jnp.zeros((F_OUT,), dtype=jnp.float32)
        return {'input': inp, 'adj': adj, 'W': W, 'b': b}
    _L1_gnn_all = _L1_gnn_setup()
    _L1_gnn_in = {k: v for k, v in _L1_gnn_all.items() if k in ('W', 'b')}
    del _L1_gnn_all
    return {'x': x, 'adj': adj, 'L0_gnn_u': _L0_gnn_in['u'], 'L1_gnn_W': _L1_gnn_in['W'], 'L1_gnn_b': _L1_gnn_in['b']}

def reference(x, adj, L0_gnn_u, L1_gnn_W, L1_gnn_b):
    import jax
    import jax.numpy as jnp

    def _L0_gnn_ref(x, adj, u):
        import jax, jax.numpy as jnp
        import numpy as np
        P_DROP = 0.1
        keep = (u >= P_DROP).astype(x.dtype)
        x_drop = x * keep / (1.0 - P_DROP)
        return jnp.matmul(adj, x_drop)

    def _L1_gnn_ref(input, adj, W, b):
        import jax, jax.numpy as jnp
        import numpy as np
        N = 8192
        F_IN = 64
        F_OUT = 64
        h = input @ W
        out = adj @ h + b
        return out
    h = jnp.maximum(_layernorm(x, axis=-1), 0.0)
    x = x + _L0_gnn_ref(h, adj, L0_gnn_u)
    h = jnp.maximum(_layernorm(x, axis=-1), 0.0)
    x = x + _L1_gnn_ref(h, adj, L1_gnn_W, L1_gnn_b)
    return x

_drawn_inputs = setup_inputs


def setup_inputs(seed=0):
    import zlib

    import numpy as np

    out = dict(_drawn_inputs(seed))
    spreads = {'L1_gnn_b': (0.0, 0.1)}
    factors = {}
    for name, (base, spread) in spreads.items():
        noise = np.random.default_rng([zlib.crc32(name.encode()), seed]).standard_normal(out[name].shape)
        drawn = base * np.exp(spread * noise) if base else spread * noise
        out[name] = jnp.asarray(drawn.astype(out[name].dtype))
    for name, factor in factors.items():
        out[name] = (out[name] * factor).astype(out[name].dtype)
    return out
```

```python
import concourse.bass as bass
from concourse import mybir
from contextlib import ExitStack


P = 128
N = 8192
D = 64
BLK = 512
BLOCKS = N // BLK
TILES = BLK // P
BAND = 2
SLOTS = 10
CHUNK_TILES = 2
CHUNKS = TILES // CHUNK_TILES
SPLIT_BUFS = 3
COPY_BUFS = 3
H2_BUFS = 3
SUM_BANKS = 6
ROW_BANKS = 2
LEAD = 5
GROUPS = [(0, 1), (1, 4), (4, 8), (8, 16)]
SCRATCH_SLOTS = 4
DROP = 0.1
EPS = 1e-05


class Unit:

    def __init__(self, kind, i, k):
        self.kind = kind
        self.i, self.k = i, k


class Sum:

    def __init__(self, kind, i):
        self.kind, self.i = kind, i


def order_of_units():
    units, row_end = [], {}
    seen = set()
    left_over = []
    for s in range(BLOCKS + 1):
        row = []
        if s < BLOCKS:
            diagonal = [Unit("one", s, k) for k in range(s, min(s + BAND + 1, BLOCKS))]
            right = [Unit("one", s, k) for k in range(s + BAND + 1, BLOCKS)]
            left = [Unit("both", s, k) for k in range(s)]
            row = diagonal + right if s == 0 else right + left[:-1] + diagonal + left[-1:]
        batches = []
        if s > 0:
            for i in range(s - BAND - 1):
                if s == BLOCKS or i % 2 == s % 2:
                    ks = [k for k in range(i + BAND + 1, s) if (i, k) not in seen]
                    seen.update((i, k) for k in ks)
                    batches.append([Unit("two", i, k) for k in ks])
            kept = [[Unit("two", i, s - 1)] for i in range(max(0, s - 1 - BAND), s)]
            batches = kept[:1] + batches[:len(batches) // 2] + kept[1:2] + batches[len(batches) // 2:] + kept[2:]
            if s == BLOCKS:
                batches.sort(key=lambda b: len(b) < 2)
        batches = [b for b in batches if b]
        lead = min(LEAD, len(row))
        spread = batches[:-1] if len(batches) > 4 and s < BLOCKS else batches
        if s == BLOCKS:
            for b in left_over + batches:
                units += b
            break
        units += [u for b in left_over for u in b]
        left_over = batches[len(spread):]
        gaps = len(row) - lead
        done = 0
        for n, u in enumerate(row):
            units.append(u)
            if n >= lead:
                due = len(spread) * (n - lead + 1) // gaps
                while done < due:
                    units += spread[done]
                    done += 1
        row_end[s] = len(units) - 1
        while units[row_end[s]].i != s or units[row_end[s]].kind == "two":
            row_end[s] -= 1
    return units, row_end


def plan():
    units, row_end = order_of_units()
    where = {}
    loads, sums = [], []
    last_use = {}
    for n, u in enumerate(units):
        u.n = n
        last_use[(u.i, u.k), u.kind == "two" and u.k > u.i + BAND] = n
    for n, u in enumerate(units):
        again = u.kind == "two" and u.k > u.i + BAND
        kept = u.kind == "two" and not again
        if kept:
            u.load = where[u.i, u.k]
        else:
            keep = u.kind == "one" and u.k <= u.i + BAND
            load = {"i": u.i, "k": u.k, "last": last_use[(u.i, u.k), False] if keep else n, "index": len(loads)}
            loads.append(load)
            where[u.i, u.k] = u.load = load
    free = [-1] * (SLOTS - SCRATCH_SLOTS) + [BLOCKS] * SCRATCH_SLOTS
    holder = [None] * SLOTS
    uses = [0] * SLOTS
    for load in loads:
        slot = min(range(SLOTS), key=lambda q: free[q])
        load["slot"], load["before"] = slot, holder[slot]
        uses[slot] += 1
        load["arrived"] = 16 * uses[slot]
        load["scratch"] = slot >= SLOTS - SCRATCH_SLOTS and holder[slot] is None
        holder[slot], free[slot] = load, load["last"]
    chunks = both = 0
    for u in units:
        u.first_chunk = chunks
        if u.kind == "both":
            both += 1
        else:
            chunks += CHUNKS
        u.chunks, u.boths = chunks, both
    open_sums = {}
    for u in units:
        if u.kind == "two":
            key = ("band", u.i) if u.k <= u.i + BAND else ("batch", u.i)
        else:
            key = (u.kind, u.i)
        if key[0] == "batch" and key in open_sums and units[open_sums[key].last + 1] is not u:
            del open_sums[key]
        if key not in open_sums:
            open_sums[key] = Sum(*key)
            open_sums[key].first = u.n
            sums.append(open_sums[key])
        u.sum = open_sums[key]
        u.sum.last = u.n
    results = []
    for s in sums:
        if s.kind in ("one", "both"):
            s.at = row_end[s.i]
        else:
            s.at = s.last
    for s, at in row_end.items():
        results.append({"at": at, "row": s, "sums": [q for q in sums if q.kind in ("one", "both") and q.i == s]})
    results += [{"at": q.at, "row": None, "i": q.i, "sums": [q]} for q in sums if q.kind not in ("one", "both")]
    results.sort(key=lambda r: r["at"])
    copies = 0
    for n, r in enumerate(results):
        r["index"] = n
        for q in sorted(r["sums"], key=lambda q: q.last):
            q.copy = copies
            q.result = n
            copies += 1
    bank_free = [(-1, None)] * SUM_BANKS
    for q in sorted(sums, key=lambda q: q.first):
        bank = min(range(SUM_BANKS), key=lambda b: bank_free[b][0])
        q.bank, q.before = bank, bank_free[bank][1]
        assert bank_free[bank][0] < q.first, "more open sums than banks"
        bank_free[bank] = (q.at, q)
    return units, loads, results


def bass_gnn(nc, x, adj, u, w, b, out):
    f32, f32r = mybir.dt.float32, mybir.dt.float32r
    ALU, ACT, AX = mybir.AluOpType, mybir.ActivationFunctionType, mybir.AxisListType

    units, loads, results = plan()
    last_result_of = {}
    for r in results:
        last_result_of[r["row"] if r["row"] is not None else r["i"]] = r["index"]
    copied = {q.copy: q for r in results for q in r["sums"]}
    last_h2_use = {t.k: t for t in units if t.kind == "two"}

    with ExitStack() as ctx:
        def sb(name, shape, dt=f32):
            return ctx.enter_context(nc.sbuf_tensor(name, shape, dt))

        def sem(name):
            return ctx.enter_context(nc.semaphore(name))

        blocks = sb("blocks", [P, SLOTS, TILES * BLK])
        adj_hi = sb("adj_hi", [P, SPLIT_BUFS, CHUNK_TILES * BLK], f32r)
        adj_lo = sb("adj_lo", [P, SPLIT_BUFS, CHUNK_TILES * BLK], f32r)
        xd_split = sb("xd_split", [P, N // P, 2 * D], f32r)
        pair = sb("pair", [P, N // P, 2 * D])
        h2_split = sb("h2_split", [P, H2_BUFS, TILES, 2 * D], f32r)
        rows = sb("rows", [P, N // P, D])
        sums_sb = sb("sums_sb", [P, COPY_BUFS, BLK])
        fold = sb("fold", [P, D])
        fold_w = sb("fold_w", [P, D])
        pair_w = sb("pair_w", [P, 2 * D])
        bias = sb("bias", [P, D])
        eps = sb("eps", [P, 1])
        total = sb("total", [P, N // P])
        square = sb("square", [P, N // P])
        dev = sb("dev", [P, N // P])
        total2 = sb("total2", [P, TILES])
        square2 = sb("square2", [P, TILES])
        dev2 = sb("dev2", [P, TILES])
        centred2 = sb("centred2", [P, TILES, D])
        squares2 = sb("squares2", [P, TILES, D])
        scratch = blocks[:, SLOTS - SCRATCH_SLOTS:SLOTS, :].rearrange("p s n -> p (s n)")
        u_sb = scratch[:, 0:N // P * D].rearrange("p (t d) -> p t d", d=D)
        centred = scratch[:, N // P * D:2 * N // P * D].rearrange("p (t d) -> p t d", d=D)

        banks = ctx.enter_context(nc.psum_tensor("banks", [P, SUM_BANKS, BLK], f32))
        row_banks = ctx.enter_context(nc.psum_tensor("row_banks", [P, ROW_BANKS, BLK], f32))

        block_arrived = [sem(f"block_arrived{n}") for n in range(SLOTS)]
        x_arrived = [sem(f"x_arrived{n}") for n in range(len(GROUPS))]
        u_arrived = [sem(f"u_arrived{n}") for n in range(len(GROUPS))]
        weights_arrived = sem("weights_arrived")
        cleared = sem("cleared")
        constants = sem("constants")
        x_step = sem("x_step")
        x_centred = sem("x_centred")
        x_squared = sem("x_squared")
        x_summed = sem("x_summed")
        x_dev = sem("x_dev")
        keep_ready = sem("keep_ready")
        keep_scaled = sem("keep_scaled")
        xd_ready = sem("xd_ready")
        xd_hi_ready = sem("xd_hi_ready")
        xd_split_ready = sem("xd_split_ready")
        adj_hi_ready = sem("adj_hi_ready")
        adj_lo_ready = sem("adj_lo_ready")
        chunk_used = sem("chunk_used")
        both_used = sem("both_used")
        sum_copied = sem("sum_copied")
        result_ready = sem("result_ready")
        result_used = sem("result_used")
        h2_step = sem("h2_step")
        h2_summed = sem("h2_summed")
        h2_dev = sem("h2_dev")
        h2_ready = sem("h2_ready")
        stored = sem("stored")
        block = ctx.enter_context(nc.Block())

        def wait_sum_complete(eng, q):
            t = units[q.last]
            if t.kind == "both":
                eng.wait_ge(both_used, t.boths)
            else:
                eng.wait_ge(chunk_used, t.chunks)

        def tiles_of(k):
            return slice(k * TILES, (k + 1) * TILES)

        @block.sync
        def _(sp):
            for load in loads:
                before = load["before"]
                if before is not None:
                    t = units[before["last"]]
                    if t.kind == "both":
                        sp.wait_ge(both_used, t.boths)
                    else:
                        sp.wait_ge(adj_lo_ready, t.chunks)
                elif load["scratch"]:
                    sp.wait_ge(xd_ready, len(GROUPS))
                sp.dma_start(blocks[:, load["slot"], :], adj[load["i"] * BLOCKS + load["k"], :, :])\
                    .then_inc(block_arrived[load["slot"]], 16)
            order = sorted(range(BLOCKS), key=lambda i: last_result_of[i])
            for i in order:
                sp.wait_ge(result_used, last_result_of[i] + 1)
                sp.dma_start(out[:, tiles_of(i), :], rows[:, tiles_of(i), :]).then_inc(stored, 16)
            sp.wait_ge(stored, 16 * BLOCKS)

        @block.gpsimd
        def _(pool):
            nc.gpsimd.memset(eps[:, :], EPS).then_inc(cleared, 1)
            nc.gpsimd.memset(fold[:, :], 0.0).then_inc(cleared, 1)
            nc.gpsimd.memset(pair_w[:, :], 0.0).then_inc(cleared, 1)
            pool.wait_ge(cleared, 3)
            nc.gpsimd.affine_select(out=fold[:, :], in_=fold[:, :], compare_op=ALU.not_equal, fill=1.0,
                                    base=0, pattern=[[-1, D]], channel_multiplier=1).then_inc(cleared, 1)
            nc.gpsimd.affine_select(out=pair_w[:, 0:D], in_=pair_w[:, 0:D], compare_op=ALU.not_equal, fill=1.0,
                                    base=0, pattern=[[-1, D]], channel_multiplier=1).then_inc(cleared, 1)
            pool.wait_ge(cleared, 5)
            nc.gpsimd.affine_select(out=fold[:, :], in_=fold[:, :], compare_op=ALU.not_equal, fill=1.0,
                                    base=-D, pattern=[[-1, D]], channel_multiplier=1).then_inc(constants, 1)
            pool.dma_start(pair_w[D:P, D:2 * D], w).then_inc(weights_arrived, 16)
            pool.dma_start(fold_w[0:D, :], w).then_inc(weights_arrived, 16)
            pool.dma_start(fold_w[D:P, :], w).then_inc(weights_arrived, 16)
            pool.dma_start(bias[:, :], b.rearrange("(a n) -> a n", a=1).to_broadcast([P, D]))\
                .then_inc(weights_arrived, 16)
            for g, (k0, k1) in enumerate(GROUPS):
                t = slice(k0 * TILES, k1 * TILES)
                pool.wait_ge(u_arrived[g], 16)
                nc.gpsimd.tensor_scalar(u_sb[:, t, :], u_sb[:, t, :], DROP, 1.0 / (1.0 - DROP),
                                        ALU.is_ge, ALU.mult).then_inc(keep_ready, 1)

        @block.scalar
        def _(act):
            for g, (k0, k1) in enumerate(GROUPS):
                t = slice(k0 * TILES, k1 * TILES)
                act.dma_start(rows[:, t, :], x[:, t, :]).then_inc(x_arrived[g], 16)
                act.dma_start(u_sb[:, t, :], u[:, t, :]).then_inc(u_arrived[g], 16)
            act.wait_ge(cleared, 1)

            def normalise(g):
                t = slice(GROUPS[g][0] * TILES, GROUPS[g][1] * TILES)
                act.wait_ge(x_centred, g + 1)
                nc.scalar.activation(pair[:, t, D:2 * D], centred[:, t, :], ACT.Square).then_inc(x_squared, 1)
                act.wait_ge(x_summed, g + 1)
                nc.scalar.activation(dev[:, t], square[:, t], ACT.Sqrt, bias=eps[:, 0:1], scale=1.0 / D)\
                    .then_inc(x_dev, 1)
                act.wait_ge(xd_ready, g + 1)
                nc.scalar.activation(xd_split[:, t, 0:D], pair[:, t, 0:D], ACT.Copy).then_inc(xd_hi_ready, 1)

            def split(t):
                act.wait_ge(block_arrived[t.load["slot"]], t.load["arrived"])
                for c in range(CHUNKS):
                    n = t.first_chunk + c
                    if n >= SPLIT_BUFS:
                        act.wait_ge(chunk_used, n - SPLIT_BUFS + 1)
                    nc.scalar.activation(adj_hi[:, n % SPLIT_BUFS, :],
                                         blocks[:, t.load["slot"], c * CHUNK_TILES * BLK:(c + 1) * CHUNK_TILES * BLK],
                                         ACT.Copy).then_inc(adj_hi_ready, 1)

            def copy_out(r):
                for q in sorted(r["sums"], key=lambda q: q.copy):
                    wait_sum_complete(act, q)
                    if q.copy >= COPY_BUFS:
                        act.wait_ge(result_ready, copied[q.copy - COPY_BUFS].result + 1)
                    nc.scalar.activation(sums_sb[:, q.copy % COPY_BUFS, :], banks[:, q.bank, :], ACT.Copy)\
                        .then_inc(sum_copied, 1)

            def deviation(s):
                act.wait_ge(h2_summed, s + 1)
                nc.scalar.activation(dev2[:, :], square2[:, :], ACT.Sqrt, bias=eps[:, 0:1], scale=1.0 / D)\
                    .then_inc(h2_dev, 1)

            for t in units + [None] * 3:
                at = t.n if t else at + 1
                if at in FIRST_UNIT_OF:
                    normalise(FIRST_UNIT_OF[at])
                if t and t.kind != "both":
                    split(t)
                for r in results:
                    if r["at"] + 1 == at:
                        copy_out(r)
                for r in results:
                    if r["at"] + 2 == at and r["row"] is not None:
                        deviation(r["row"])

        @block.vector
        def _(dve):
            steps = [0]

            def link(semaphore, instruction):
                steps[0] += 1
                instruction.then_inc(semaphore, 1)
                dve.wait_ge(semaphore, steps[0])

            def normalise(g):
                k0, k1 = GROUPS[g]
                t = slice(k0 * TILES, k1 * TILES)
                shape = [P, (k1 - k0) * TILES, D]
                dve.wait_ge(x_arrived[g], 16)
                link(x_step, nc.vector.tensor_reduce(total[:, t], rows[:, t, :], AX.X, ALU.add))
                link(x_step, nc.vector.tensor_scalar(total[:, t], total[:, t], -1.0 / D, None, ALU.mult))
                nc.vector.tensor_tensor(centred[:, t, :], rows[:, t, :], total[:, t].unsqueeze(2).to_broadcast(shape),
                                        ALU.add).then_inc(x_centred, 1)
                dve.wait_ge(x_squared, g + 1)
                nc.vector.tensor_reduce(square[:, t], pair[:, t, D:2 * D], AX.X, ALU.add).then_inc(x_summed, 1)
                dve.wait_ge(x_dev, g + 1)
                link(x_step, nc.vector.reciprocal(square[:, t], dev[:, t]))
                dve.wait_ge(keep_ready, g + 1)
                link(x_step, nc.vector.scalar_tensor_tensor(
                    out=centred[:, t, :], in0=centred[:, t, :], scalar=0.0,
                    in1=square[:, t].unsqueeze(2).to_broadcast(shape), op0=ALU.max, op1=ALU.mult))
                nc.vector.tensor_tensor(pair[:, t, 0:D], centred[:, t, :], u_sb[:, t, :], ALU.mult)\
                    .then_inc(xd_ready, 1)
                dve.wait_ge(xd_hi_ready, g + 1)
                nc.vector.tensor_tensor(xd_split[:, t, D:2 * D], pair[:, t, 0:D], xd_split[:, t, 0:D].bitcast(f32),
                                        ALU.subtract).then_inc(xd_split_ready, 1)

            def split(t):
                for c in range(CHUNKS):
                    n = t.first_chunk + c
                    dve.wait_ge(adj_hi_ready, n + 1)
                    nc.vector.tensor_tensor(adj_lo[:, n % SPLIT_BUFS, :],
                                            blocks[:, t.load["slot"], c * CHUNK_TILES * BLK:(c + 1) * CHUNK_TILES * BLK],
                                            adj_hi[:, n % SPLIT_BUFS, :].bitcast(f32), ALU.subtract)\
                        .then_inc(adj_lo_ready, 1)

            h2_steps = [0]

            def link2(instruction):
                h2_steps[0] += 1
                instruction.then_inc(h2_step, 1)
                dve.wait_ge(h2_step, h2_steps[0])

            def row_of_layer_1(r):
                s = r["row"]
                shape = [P, TILES, D]
                mine = rows[:, tiles_of(s), :]
                bank = row_banks[:, r["index"] % ROW_BANKS, :].rearrange("p (t e) -> p t e", e=2 * D)
                dve.wait_ge(result_ready, r["index"] + 1)
                link2(nc.vector.tensor_tensor(mine, mine, bank[:, :, 0:D], ALU.add))
                link2(nc.vector.tensor_reduce(total2[:, :], mine, AX.X, ALU.add))
                link2(nc.vector.tensor_scalar(total2[:, :], total2[:, :], -1.0 / D, None, ALU.mult))
                link2(nc.vector.tensor_tensor(centred2[:, :, :], mine, total2[:, :].unsqueeze(2).to_broadcast(shape),
                                              ALU.add))
                link2(nc.vector.tensor_tensor(squares2[:, :, :], centred2[:, :, :], centred2[:, :, :], ALU.mult))
                nc.vector.tensor_reduce(square2[:, :], squares2[:, :, :], AX.X, ALU.add).then_inc(h2_summed, 1)
                if s > 0:
                    link2(nc.vector.tensor_tensor(mine, mine, bank[:, :, D:2 * D], ALU.add))
                dve.wait_ge(weights_arrived, 64)
                nc.vector.tensor_tensor(mine, mine, bias[:, :].unsqueeze(1).to_broadcast(shape), ALU.add)\
                    .then_inc(result_used, 1)
                dve.wait_ge(h2_dev, s + 1)
                link2(nc.vector.reciprocal(square2[:, :], dev2[:, :]))
                h2 = pair[:, tiles_of(s), D:2 * D]
                split_h2 = h2_split[:, s % H2_BUFS, :, :]
                link2(nc.vector.scalar_tensor_tensor(
                    out=h2, in0=centred2[:, :, :], scalar=0.0,
                    in1=square2[:, :].unsqueeze(2).to_broadcast(shape), op0=ALU.max, op1=ALU.mult))
                if s >= H2_BUFS:
                    dve.wait_ge(chunk_used, last_h2_use[s - H2_BUFS].chunks)
                link2(nc.vector.tensor_copy(split_h2[:, :, 0:D], h2))
                nc.vector.tensor_tensor(split_h2[:, :, D:2 * D], h2, split_h2[:, :, 0:D].bitcast(f32),
                                        ALU.subtract).then_inc(h2_ready, 1)

            def part_of_layer_2(r):
                mine = rows[:, tiles_of(r["i"]), :]
                bank = row_banks[:, r["index"] % ROW_BANKS, 0:TILES * D].rearrange("p (t d) -> p t d", d=D)
                dve.wait_ge(result_ready, r["index"] + 1)
                if r["index"] >= 1:
                    dve.wait_ge(result_used, r["index"])
                nc.vector.tensor_tensor(mine, mine, bank, ALU.add).then_inc(result_used, 1)

            for t in units + [None] * 3:
                at = t.n if t else at + 1
                if at in FIRST_UNIT_OF:
                    normalise(FIRST_UNIT_OF[at])
                if t and t.kind != "both":
                    split(t)
                for r in results:
                    if r["at"] + 2 == at:
                        if r["row"] is not None:
                            row_of_layer_1(r)
                        else:
                            part_of_layer_2(r)

        @block.tensor
        def _(pe):
            def multiply(t):
                q = t.sum
                bank = banks[:, q.bank, :]
                first, last = t.n == q.first, t.n == q.last
                if first and q.before is not None:
                    pe.wait_ge(sum_copied, q.before.copy + 1)
                if t.kind == "one" and t.i == 0:
                    pe.wait_ge(xd_split_ready, GROUP_OF[t.k] + 1)
                if t.kind != "one":
                    pe.wait_ge(h2_ready, t.k + 1)
                if t.kind == "both":
                    pe.wait_ge(block_arrived[t.load["slot"]], t.load["arrived"])
                    for j in range(TILES):
                        done = nc.tensor.matmul(bank, pair[:, t.k * TILES + j, :],
                                                blocks[:, t.load["slot"], j * BLK:(j + 1) * BLK],
                                                start=first and j == 0, stop=last and j == TILES - 1)
                    done.then_inc(both_used, 1)
                    return
                for c in range(CHUNKS):
                    n = t.first_chunk + c
                    pe.wait_ge(adj_lo_ready, n + 1)
                    for jj in range(CHUNK_TILES):
                        j = c * CHUNK_TILES + jj
                        if t.kind == "one":
                            features = xd_split[:, t.k * TILES + j, :]
                        else:
                            features = h2_split[:, t.k % H2_BUFS, j, :]
                        cols = slice(jj * BLK, (jj + 1) * BLK)
                        nc.tensor.matmul(bank, features, adj_hi[:, n % SPLIT_BUFS, cols],
                                         start=first and j == 0, stop=False)
                        done = nc.tensor.matmul(bank, features, adj_lo[:, n % SPLIT_BUFS, cols],
                                                start=False, stop=last and j == TILES - 1)
                    done.then_inc(chunk_used, 1)

            def transpose_out(r):
                if r["index"] == 0:
                    pe.wait_ge(constants, 1)
                    pe.wait_ge(cleared, 5)
                    pe.wait_ge(weights_arrived, 64)
                if r["index"] >= ROW_BANKS:
                    pe.wait_ge(result_used, r["index"] - ROW_BANKS + 1)
                for q in r["sums"]:
                    pe.wait_ge(sum_copied, q.copy + 1)
                bank = row_banks[:, r["index"] % ROW_BANKS, :]
                of = {q.kind: sums_sb[:, q.copy % COPY_BUFS, :] for q in r["sums"]}
                for j in range(TILES):
                    cols = slice(j * P, (j + 1) * P)
                    if r["row"] is None:
                        [only] = of.values()
                        done = nc.tensor.matmul(bank[:, j * D:(j + 1) * D], only[:, cols], fold_w[:, :],
                                                start=True, stop=True)
                    else:
                        at = j * 2 * D
                        if "both" in of:
                            nc.tensor.matmul(bank[:, at:at + 2 * D], of["both"][:, cols], pair_w[:, :],
                                             start=True, stop=False)
                        done = nc.tensor.matmul(bank[:, at:at + D], of["one"][:, cols], fold[:, :],
                                                start="both" not in of, stop=True)
                done.then_inc(result_ready, 1)

            for t in units + [None] * 3:
                at = t.n if t else at + 1
                if t:
                    multiply(t)
                for r in results:
                    if r["at"] + 1 == at:
                        transpose_out(r)


FIRST_UNIT_OF = {k0 - 1 if k0 > 1 else k0: g for g, (k0, k1) in enumerate(GROUPS)}
GROUP_OF = {k: g for g, (k0, k1) in enumerate(GROUPS) for k in range(k0, k1)}


def kernel(x, adj, L0_gnn_u, L1_gnn_W, L1_gnn_b):
    import numpy as np
    import concourse.bacc as bacc
    from concourse.bass_utils import run_bass_kernel_spmd

    def by_partition(a):
        return np.ascontiguousarray(np.asarray(a).reshape(N // P, P, D).transpose(1, 0, 2))

    blocks = np.ascontiguousarray(
        np.asarray(adj).reshape(BLOCKS, BLK, BLOCKS, TILES, P).transpose(0, 2, 4, 3, 1)
    ).reshape(BLOCKS * BLOCKS, P, TILES * BLK)
    arrays = {"x": by_partition(x), "adj": blocks, "u": by_partition(L0_gnn_u),
              "w": np.ascontiguousarray(L1_gnn_W), "b": np.ascontiguousarray(L1_gnn_b)}
    nc = bacc.Bacc("TRN2", target_bir_lowering=False, num_devices=1)
    args = [nc.dram_tensor(f"in_{name}", a.shape, mybir.dt.from_np(a.dtype), kind="ExternalInput").ap()
            for name, a in arrays.items()]
    out = nc.dram_tensor("out", (P, N // P, D), mybir.dt.float32, kind="ExternalOutput").ap()
    bass_gnn(nc, *args, out)
    r = run_bass_kernel_spmd(nc, [{f"in_{name}": a for name, a in arrays.items()}], core_ids=[0])
    return np.ascontiguousarray(r.results[0]["out"].transpose(1, 0, 2)).reshape(N, D)
```

```python
import concourse.bass as bass
from concourse import mybir
from contextlib import ExitStack


P = 128
N = 8192
D = 64
BLK = 512
BLOCKS = N // BLK
TILES = BLK // P
BAND = 2
SLOTS = 12
CHUNK_TILES = 1
CHUNKS = TILES // CHUNK_TILES
SPLIT_BUFS = 9
COPY_BUFS = 3
H2_BUFS = 3
PAIR_BUFS = 2
SUM_BANKS = 6
ROW_BANKS = 2
CHAIN = 3
LEAD = 5
FIRST_WHOLE = 2
LAST_STAGES = 1
GROUPS = [(0, 1), (1, 2)] + [(k, k + 2) for k in range(2, BLOCKS, 2)]
SCRATCH_SLOTS = 4
DROP = 0.1
EPS = 1e-05


class Unit:

    def __init__(self, kind, i, k):
        self.kind = kind
        self.unsplit = kind in ("plain", "both")
        self.i, self.k = i, k


class Sum:

    def __init__(self, kind, i):
        self.kind, self.i = kind, i


def order_of_units():
    units, row_end = [], {}
    seen = set()
    behind = []
    for s in range(BLOCKS + 1):
        split, whole, last = [], [], []
        if s < BLOCKS:
            split = [Unit("one", s, k) for k in range(s + BAND + 1, BLOCKS)]
            split += [Unit("one", s, k) for k in range(s, min(s + BAND + 1, BLOCKS))]
            whole = [Unit("both", s, k) for k in range(s)]
            whole, last = whole[:-1], whole[-1:]
            if s == 0:
                split = [Unit("plain" if k % 2 else "one", 0, k) for k in range(BLOCKS)]
        first, whole = whole[:FIRST_WHOLE], whole[FIRST_WHOLE:]
        again = []
        for i in range(s - BAND - 1):
            if s >= BLOCKS - LAST_STAGES or i % 2 == s % 2:
                ks = [k for k in range(i + BAND + 1, s) if (i, k) not in seen]
                seen.update((i, k) for k in ks)
                again.append([Unit("two", i, k) for k in ks])
        kept = [[Unit("two", i, s - 1)] for i in range(max(0, s - 1 - BAND), s)] if s else []
        half = len(again) // 2
        second = kept[:1] + again[:half] + kept[1:2] + again[half:] + kept[2:]
        second = [q for q in second if q]
        if s == BLOCKS:
            for batch in behind + second:
                units += batch
            break
        now = second[:-1] if len(second) > 3 else second
        start = max(0, LEAD - len(first)) / (len(split) + len(whole) + len(now))
        mixed = [((n + 0.5) / len(split), [t]) for n, t in enumerate(split)]
        mixed += [(n / len(whole), [t]) for n, t in enumerate(whole)]
        mixed += [(start + (1 - start) * (n + 0.5) / len(now), batch) for n, batch in enumerate(now)]
        units += first
        for batch in behind:
            units += batch
        for _, batch in sorted(mixed, key=lambda m: m[0]):
            units += batch
        units += last
        behind = second[len(now):]
        row_end[s] = max(n for n, t in enumerate(units) if t.i == s and t.kind != "two")
    return units, row_end


def plan():
    units, row_end = order_of_units()
    where = {}
    loads, sums = [], []
    last_use = {}
    for n, u in enumerate(units):
        u.n = n
        last_use[(u.i, u.k), u.kind == "two" and u.k > u.i + BAND] = n
    for n, u in enumerate(units):
        again = u.kind == "two" and u.k > u.i + BAND
        kept = u.kind == "two" and not again
        if kept:
            u.load = where[u.i, u.k]
        else:
            keep = u.kind in ("one", "plain") and u.k <= u.i + BAND
            load = {"i": u.i, "k": u.k, "last": last_use[(u.i, u.k), False] if keep else n, "index": len(loads)}
            loads.append(load)
            where[u.i, u.k] = u.load = load
    free = [-1] * (SLOTS - SCRATCH_SLOTS) + [BLOCKS] * SCRATCH_SLOTS
    holder = [None] * SLOTS
    uses = [0] * SLOTS
    for load in loads:
        slot = min(range(SLOTS), key=lambda q: free[q])
        load["slot"], load["before"] = slot, holder[slot]
        uses[slot] += 1
        load["arrived"] = 16 * uses[slot]
        load["scratch"] = slot >= SLOTS - SCRATCH_SLOTS and holder[slot] is None
        holder[slot], free[slot] = load, load["last"]
    chunks = unsplits = 0
    for u in units:
        u.first_chunk = chunks
        if u.unsplit:
            unsplits += 1
        else:
            chunks += CHUNKS
        u.chunks, u.unsplits = chunks, unsplits
    open_sums = {}
    for u in units:
        if u.kind == "two":
            key = ("band", u.i) if u.k <= u.i + BAND else ("batch", u.i)
        else:
            key = (u.kind, u.i)
        if key[0] == "batch" and key in open_sums and units[open_sums[key].last + 1] is not u:
            del open_sums[key]
        if key not in open_sums:
            open_sums[key] = Sum(*key)
            open_sums[key].first = u.n
            sums.append(open_sums[key])
        u.sum = open_sums[key]
        u.sum.last = u.n
    results = []
    for s in sums:
        if s.kind in ("one", "plain", "both"):
            s.at = row_end[s.i]
        else:
            s.at = s.last
    for s, at in row_end.items():
        results.append({"at": at, "row": s, "sums": [q for q in sums if q.kind in ("one", "plain", "both") and q.i == s]})
    results += [{"at": q.at, "row": None, "i": q.i, "sums": [q]} for q in sums if q.kind not in ("one", "plain", "both")]
    results.sort(key=lambda r: r["at"])
    taken = 0
    for r in results:
        taken = r["taken"] = max(taken, r["at"] + (2 if r["row"] in (None, BLOCKS - 1) else CHAIN))
    copies = 0
    for n, r in enumerate(results):
        r["index"] = n
        for q in sorted(r["sums"], key=lambda q: q.last):
            q.copy = copies
            q.result = n
            copies += 1
    bank_free = [(-1, None)] * SUM_BANKS
    for q in sorted(sums, key=lambda q: q.first):
        bank = min(range(SUM_BANKS), key=lambda b: bank_free[b][0])
        q.bank, q.before = bank, bank_free[bank][1]
        assert bank_free[bank][0] < q.first, "more open sums than banks"
        bank_free[bank] = (q.at, q)
    return units, loads, results


def bass_gnn(nc, x, adj, u, w, b, out):
    f32, f32r = mybir.dt.float32, mybir.dt.float32r
    ALU, ACT, AX = mybir.AluOpType, mybir.ActivationFunctionType, mybir.AxisListType

    units, loads, results = plan()
    last_result_of = {}
    for r in results:
        last_result_of[r["row"] if r["row"] is not None else r["i"]] = r["index"]
    copied = {q.copy: q for r in results for q in r["sums"]}
    last_h2_use = {t.k: t for t in units if t.kind == "two"}

    with ExitStack() as ctx:
        def sb(name, shape, dt=f32):
            return ctx.enter_context(nc.sbuf_tensor(name, shape, dt))

        def sem(name):
            return ctx.enter_context(nc.semaphore(name))

        blocks = sb("blocks", [P, SLOTS, TILES * BLK])
        adj_hi = sb("adj_hi", [P, SPLIT_BUFS, CHUNK_TILES * BLK], f32r)
        adj_lo = sb("adj_lo", [P, SPLIT_BUFS, CHUNK_TILES * BLK], f32r)
        features = sb("features", [P, N // P, 2 * D], f32r)
        pair = sb("pair", [P, PAIR_BUFS, TILES, 2 * D])
        h2_split = sb("h2_split", [P, H2_BUFS, TILES, 2 * D], f32r)
        rows = sb("rows", [P, N // P, D])
        sums_sb = sb("sums_sb", [P, COPY_BUFS, BLK])
        fold = sb("fold", [P, D])
        fold_w = sb("fold_w", [P, D])
        pair_w = sb("pair_w", [P, 2 * D])
        bias = sb("bias", [P, D])
        eps = sb("eps", [P, 1])
        total = sb("total", [P, N // P])
        square = sb("square", [P, N // P])
        dev = sb("dev", [P, N // P])
        total2 = sb("total2", [P, TILES])
        square2 = sb("square2", [P, TILES])
        dev2 = sb("dev2", [P, TILES])
        centred2 = sb("centred2", [P, TILES, D])
        squares2 = sb("squares2", [P, TILES, D])
        scratch = blocks[:, SLOTS - SCRATCH_SLOTS:SLOTS, :].rearrange("p s n -> p (s n)")
        u_sb = scratch[:, 0:N // P * D].rearrange("p (t d) -> p t d", d=D)
        centred = scratch[:, N // P * D:2 * N // P * D].rearrange("p (t d) -> p t d", d=D)

        x_squares = sums_sb[:, :, :].rearrange("p b (t d) -> p b t d", d=D)

        banks = ctx.enter_context(nc.psum_tensor("banks", [P, SUM_BANKS, BLK], f32))
        row_banks = ctx.enter_context(nc.psum_tensor("row_banks", [P, ROW_BANKS, BLK], f32))

        block_arrived = [sem(f"block_arrived{n}") for n in range(SLOTS)]
        x_arrived = [sem(f"x_arrived{n}") for n in range(len(GROUPS))]
        u_arrived = [sem(f"u_arrived{n}") for n in range(len(GROUPS))]
        weights_arrived = sem("weights_arrived")
        cleared = sem("cleared")
        constants = sem("constants")
        x_step = sem("x_step")
        warm = sem("warm")
        x_centred = sem("x_centred")
        x_squared = sem("x_squared")
        x_summed = sem("x_summed")
        x_dev = sem("x_dev")
        x_scale = sem("x_scale")
        keep_ready = sem("keep_ready")
        keep_scaled = sem("keep_scaled")
        xd_ready = sem("xd_ready")
        xd_hi_ready = sem("xd_hi_ready")
        xd_split_ready = sem("xd_split_ready")
        adj_hi_ready = sem("adj_hi_ready")
        adj_lo_ready = sem("adj_lo_ready")
        chunk_used = sem("chunk_used")
        unsplit_used = sem("unsplit_used")
        sum_copied = sem("sum_copied")
        result_ready = sem("result_ready")
        result_used = sem("result_used")
        h2_step = sem("h2_step")
        h2_summed = sem("h2_summed")
        h2_dev = sem("h2_dev")
        h2_ready = sem("h2_ready")
        pair_ready = sem("pair_ready")
        pair_arrived = sem("pair_arrived")
        stored = sem("stored")
        block = ctx.enter_context(nc.Block())

        def wait_sum_complete(eng, q):
            t = units[q.last]
            if t.unsplit:
                eng.wait_ge(unsplit_used, t.unsplits)
            else:
                eng.wait_ge(chunk_used, t.chunks)

        def tiles_of(k):
            return slice(k * TILES, (k + 1) * TILES)

        @block.sync
        def _(sp):
            t = slice(0, GROUPS[0][1] * TILES)
            sp.dma_start(rows[:, t, :], x[:, t, :]).then_inc(x_arrived[0], 16)
            sp.dma_start(u_sb[:, t, :], u[:, t, :]).then_inc(u_arrived[0], 16)
            for load in loads:
                before = load["before"]
                if before is not None:
                    t = units[before["last"]]
                    if t.unsplit:
                        sp.wait_ge(unsplit_used, t.unsplits)
                    else:
                        sp.wait_ge(adj_lo_ready, t.chunks)
                elif load["scratch"]:
                    sp.wait_ge(xd_split_ready, len(GROUPS))
                    sp.wait_ge(unsplit_used, units[BLOCKS - 1].unsplits)
                sp.dma_start(blocks[:, load["slot"], :], adj[load["i"] * BLOCKS + load["k"], :, :])\
                    .then_inc(block_arrived[load["slot"]], 16)
            order = sorted(range(BLOCKS), key=lambda i: last_result_of[i])
            for i in order:
                sp.wait_ge(result_used, last_result_of[i] + 1)
                sp.dma_start(out[:, tiles_of(i), :], rows[:, tiles_of(i), :]).then_inc(stored, 16)
            sp.wait_ge(stored, 16 * BLOCKS)

        @block.gpsimd
        def _(pool):
            nc.gpsimd.memset(eps[:, :], EPS).then_inc(cleared, 1)
            nc.gpsimd.memset(fold[:, :], 0.0).then_inc(cleared, 1)
            nc.gpsimd.memset(pair_w[:, :], 0.0).then_inc(cleared, 1)
            pool.wait_ge(cleared, 3)
            nc.gpsimd.affine_select(out=fold[:, :], in_=fold[:, :], compare_op=ALU.not_equal, fill=1.0,
                                    base=0, pattern=[[-1, D]], channel_multiplier=1).then_inc(cleared, 1)
            nc.gpsimd.affine_select(out=pair_w[:, 0:D], in_=pair_w[:, 0:D], compare_op=ALU.not_equal, fill=1.0,
                                    base=0, pattern=[[-1, D]], channel_multiplier=1).then_inc(cleared, 1)
            pool.wait_ge(cleared, 5)
            nc.gpsimd.affine_select(out=fold[:, :], in_=fold[:, :], compare_op=ALU.not_equal, fill=1.0,
                                    base=-D, pattern=[[-1, D]], channel_multiplier=1).then_inc(constants, 1)
            pool.dma_start(pair_w[D:P, D:2 * D], w).then_inc(weights_arrived, 16)
            pool.dma_start(fold_w[0:D, :], w).then_inc(weights_arrived, 16)
            pool.dma_start(fold_w[D:P, :], w).then_inc(weights_arrived, 16)
            pool.dma_start(bias[:, :], b.rearrange("(a n) -> a n", a=1).to_broadcast([P, D]))\
                .then_inc(weights_arrived, 16)
            for g, (k0, k1) in enumerate(GROUPS):
                t = slice(k0 * TILES, k1 * TILES)
                pool.wait_ge(u_arrived[g], 16)
                nc.gpsimd.tensor_scalar(u_sb[:, t, :], u_sb[:, t, :], DROP, 1.0 / (1.0 - DROP),
                                        ALU.is_ge, ALU.mult).then_inc(keep_ready, 1)
                pool.wait_ge(keep_ready, g + 1)
                pool.wait_ge(x_scale, g + 1)
                shape = [P, (k1 - k0) * TILES, D]
                nc.gpsimd.tensor_tensor(u_sb[:, t, :], u_sb[:, t, :], square[:, t].unsqueeze(2).to_broadcast(shape),
                                        ALU.mult).then_inc(keep_scaled, 1)

        @block.scalar
        def _(act):
            for g, (k0, k1) in list(enumerate(GROUPS))[1:]:
                t = slice(k0 * TILES, k1 * TILES)
                act.dma_start(rows[:, t, :], x[:, t, :]).then_inc(x_arrived[g], 16)
                act.dma_start(u_sb[:, t, :], u[:, t, :]).then_inc(u_arrived[g], 16)
            act.wait_ge(cleared, 1)

            def square_x(g):
                t = slice(GROUPS[g][0] * TILES, GROUPS[g][1] * TILES)
                act.wait_ge(x_centred, g + 1)
                n = t.stop - t.start
                nc.scalar.activation(x_squares[:, g % COPY_BUFS, 0:n, :], centred[:, t, :], ACT.Square)\
                    .then_inc(x_squared, 1)

            def deviation_x(g):
                t = slice(GROUPS[g][0] * TILES, GROUPS[g][1] * TILES)
                act.wait_ge(x_summed, g + 1)
                nc.scalar.activation(dev[:, t], square[:, t], ACT.Sqrt, bias=eps[:, 0:1], scale=1.0 / D)\
                    .then_inc(x_dev, 1)

            def xd_hi(g):
                t = slice(GROUPS[g][0] * TILES, GROUPS[g][1] * TILES)
                act.wait_ge(xd_ready, g + 1)
                nc.scalar.activation(features[:, t, 0:D], centred[:, t, :], ACT.Copy).then_inc(xd_hi_ready, 1)

            def split(t, chunks=range(CHUNKS)):
                act.wait_ge(block_arrived[t.load["slot"]], t.load["arrived"])
                for c in chunks:
                    n = t.first_chunk + c
                    if n >= SPLIT_BUFS:
                        act.wait_ge(chunk_used, n - SPLIT_BUFS + 1)
                    nc.scalar.activation(adj_hi[:, n % SPLIT_BUFS, :],
                                         blocks[:, t.load["slot"], c * CHUNK_TILES * BLK:(c + 1) * CHUNK_TILES * BLK],
                                         ACT.Copy).then_inc(adj_hi_ready, 1)

            def copy_out(r):
                for q in sorted(r["sums"], key=lambda q: q.copy):
                    wait_sum_complete(act, q)
                    if q.copy >= COPY_BUFS:
                        act.wait_ge(result_ready, copied[q.copy - COPY_BUFS].result + 1)
                    height = D if q.kind == "plain" else P
                    nc.scalar.activation(sums_sb[0:height, q.copy % COPY_BUFS, :], banks[0:height, q.bank, :], ACT.Copy)\
                        .then_inc(sum_copied, 1)

            def place_pair(s):
                act.wait_ge(h2_ready, s + 1)
                act.wait_ge(pair_ready, s + 1)
                act.dma_start(features[:, tiles_of(s), :].bitcast(f32), pair[:, s % PAIR_BUFS, :, :])\
                    .then_inc(pair_arrived, 16)

            def deviation(s):
                act.wait_ge(h2_summed, s + 1)
                nc.scalar.activation(dev2[:, :], square2[:, :], ACT.Sqrt, bias=eps[:, 0:1], scale=1.0 / D)\
                    .then_inc(h2_dev, 1)

            nc.scalar.activation(dev[:, 0:1], eps[:, 0:1], ACT.Sqrt).then_inc(warm, 1)
            act.wait_ge(warm, 1)
            for g in range(len(GROUPS) + 1):
                ahead = [t for t in units[:BLOCKS] if g and GROUP_OF[t.k] == g - 1 and not t.unsplit]
                for t in ahead:
                    split(t, range(CHUNKS // 2))
                if g < len(GROUPS):
                    square_x(g)
                for t in ahead:
                    split(t, range(CHUNKS // 2, CHUNKS))
                if g < len(GROUPS):
                    deviation_x(g)
                if g:
                    xd_hi(g - 1)

            for t in units[BLOCKS:] + [None] * 4:
                at = t.n if t else at + 1
                if t and not t.unsplit:
                    split(t)
                for r in results:
                    if r["at"] + 1 == at:
                        copy_out(r)
                for r in results:
                    if r["taken"] == at and r["row"] is not None:
                        deviation(r["row"])
                    if r["taken"] + 2 == at and r["row"] is not None and r["row"] < BLOCKS - 1:
                        place_pair(r["row"])

        @block.vector
        def _(dve):
            steps = [0]

            def link(semaphore, instruction):
                steps[0] += 1
                instruction.then_inc(semaphore, 1)
                dve.wait_ge(semaphore, steps[0])

            def tiles_of_group(g):
                k0, k1 = GROUPS[g]
                return slice(k0 * TILES, k1 * TILES), [P, (k1 - k0) * TILES, D]

            def centre_x(g):
                t, shape = tiles_of_group(g)
                dve.wait_ge(x_arrived[g], 16)
                link(x_step, nc.vector.tensor_reduce(total[:, t], rows[:, t, :], AX.X, ALU.add))
                link(x_step, nc.vector.tensor_scalar(total[:, t], total[:, t], -1.0 / D, None, ALU.mult))
                nc.vector.tensor_tensor(centred[:, t, :], rows[:, t, :], total[:, t].unsqueeze(2).to_broadcast(shape),
                                        ALU.add).then_inc(x_centred, 1)

            def sum_squares_x(g):
                t, _ = tiles_of_group(g)
                dve.wait_ge(x_squared, g + 1)
                n = t.stop - t.start
                nc.vector.tensor_reduce(square[:, t], x_squares[:, g % COPY_BUFS, 0:n, :], AX.X, ALU.add)\
                    .then_inc(x_summed, 1)

            def scale_x(g):
                t, _ = tiles_of_group(g)
                dve.wait_ge(x_dev, g + 1)
                nc.vector.reciprocal(square[:, t], dev[:, t]).then_inc(x_scale, 1)

            def drop_x(g):
                t, _ = tiles_of_group(g)
                dve.wait_ge(keep_scaled, g + 1)
                nc.vector.scalar_tensor_tensor(out=centred[:, t, :], in0=centred[:, t, :], scalar=0.0,
                                               in1=u_sb[:, t, :], op0=ALU.max, op1=ALU.mult).then_inc(xd_ready, 1)

            def xd_lo(g):
                t, _ = tiles_of_group(g)
                dve.wait_ge(xd_hi_ready, g + 1)
                nc.vector.tensor_tensor(features[:, t, D:2 * D], centred[:, t, :], features[:, t, 0:D].bitcast(f32),
                                        ALU.subtract).then_inc(xd_split_ready, 1)

            def split(t, chunks=range(CHUNKS)):
                for c in chunks:
                    n = t.first_chunk + c
                    dve.wait_ge(adj_hi_ready, n + 1)
                    nc.vector.tensor_tensor(adj_lo[:, n % SPLIT_BUFS, :],
                                            blocks[:, t.load["slot"], c * CHUNK_TILES * BLK:(c + 1) * CHUNK_TILES * BLK],
                                            adj_hi[:, n % SPLIT_BUFS, :].bitcast(f32), ALU.subtract)\
                        .then_inc(adj_lo_ready, 1)

            h2_steps = [0]

            def link2(instruction):
                h2_steps[0] += 1
                instruction.then_inc(h2_step, 1)
                dve.wait_ge(h2_step, h2_steps[0])

            def row_of_layer_1(r):
                s = r["row"]
                shape = [P, TILES, D]
                mine = rows[:, tiles_of(s), :]
                bank = row_banks[:, r["index"] % ROW_BANKS, :].rearrange("p (t e) -> p t e", e=2 * D)
                dve.wait_ge(result_ready, r["index"] + 1)
                link2(nc.vector.tensor_tensor(mine, mine, bank[:, :, 0:D], ALU.add))
                link2(nc.vector.tensor_reduce(total2[:, :], mine, AX.X, ALU.add))
                link2(nc.vector.tensor_scalar(total2[:, :], total2[:, :], -1.0 / D, None, ALU.mult))
                link2(nc.vector.tensor_tensor(centred2[:, :, :], mine, total2[:, :].unsqueeze(2).to_broadcast(shape),
                                              ALU.add))
                link2(nc.vector.tensor_tensor(squares2[:, :, :], centred2[:, :, :], centred2[:, :, :], ALU.mult))
                nc.vector.tensor_reduce(square2[:, :], squares2[:, :, :], AX.X, ALU.add).then_inc(h2_summed, 1)
                if s > 0:
                    link2(nc.vector.tensor_tensor(mine, mine, bank[:, :, D:2 * D], ALU.add))
                dve.wait_ge(weights_arrived, 64)
                nc.vector.tensor_tensor(mine, mine, bias[:, :].unsqueeze(1).to_broadcast(shape), ALU.add)\
                    .then_inc(result_used, 1)
                dve.wait_ge(h2_dev, s + 1)
                link2(nc.vector.reciprocal(square2[:, :], dev2[:, :]))
                h2 = pair[:, s % PAIR_BUFS, :, D:2 * D]
                split_h2 = h2_split[:, s % H2_BUFS, :, :]
                if s >= PAIR_BUFS:
                    dve.wait_ge(pair_arrived, 16 * (s - PAIR_BUFS + 1))
                link2(nc.vector.scalar_tensor_tensor(
                    out=h2, in0=centred2[:, :, :], scalar=0.0,
                    in1=square2[:, :].unsqueeze(2).to_broadcast(shape), op0=ALU.max, op1=ALU.mult))
                if s >= H2_BUFS:
                    dve.wait_ge(chunk_used, last_h2_use[s - H2_BUFS].chunks)
                link2(nc.vector.tensor_copy(split_h2[:, :, 0:D], h2))
                nc.vector.tensor_tensor(split_h2[:, :, D:2 * D], h2, split_h2[:, :, 0:D].bitcast(f32),
                                        ALU.subtract).then_inc(h2_ready, 1)
                if s < BLOCKS - 1:
                    mine = features[:, tiles_of(s), :].bitcast(f32)
                    nc.vector.tensor_tensor(pair[:, s % PAIR_BUFS, :, 0:D], mine[:, :, 0:D], mine[:, :, D:2 * D],
                                            ALU.add).then_inc(pair_ready, 1)

            def part_of_layer_2(r):
                mine = rows[:, tiles_of(r["i"]), :]
                bank = row_banks[:, r["index"] % ROW_BANKS, 0:TILES * D].rearrange("p (t d) -> p t d", d=D)
                dve.wait_ge(result_ready, r["index"] + 1)
                if r["index"] >= 1:
                    dve.wait_ge(result_used, r["index"])
                nc.vector.tensor_tensor(mine, mine, bank, ALU.add).then_inc(result_used, 1)

            for g in range(len(GROUPS) + 1):
                ahead = [t for t in units[:BLOCKS] if g and GROUP_OF[t.k] == g - 1 and not t.unsplit]
                if g < len(GROUPS):
                    centre_x(g)
                if g:
                    scale_x(g - 1)
                for t in ahead:
                    split(t, range(CHUNKS // 2))
                if g < len(GROUPS):
                    sum_squares_x(g)
                if g:
                    drop_x(g - 1)
                for t in ahead:
                    split(t, range(CHUNKS // 2, CHUNKS))
                if g:
                    xd_lo(g - 1)

            for t in units[BLOCKS:] + [None] * 4:
                at = t.n if t else at + 1
                if t and not t.unsplit:
                    split(t)
                for r in results:
                    if r["taken"] == at:
                        if r["row"] is not None:
                            row_of_layer_1(r)
                        else:
                            part_of_layer_2(r)

        @block.tensor
        def _(pe):
            def multiply(t):
                q = t.sum
                bank = banks[:, q.bank, :]
                first, last = t.n == q.first, t.n == q.last
                if first and q.before is not None:
                    pe.wait_ge(sum_copied, q.before.copy + 1)
                if t.kind == "one" and t.i == 0:
                    pe.wait_ge(xd_split_ready, GROUP_OF[t.k] + 1)
                if t.kind == "plain":
                    pe.wait_ge(xd_ready, GROUP_OF[t.k] + 1)
                if t.kind == "two":
                    pe.wait_ge(h2_ready, t.k + 1)
                if t.unsplit:
                    pe.wait_ge(block_arrived[t.load["slot"]], t.load["arrived"])
                    if t.kind == "both":
                        pe.wait_ge(pair_arrived, 16 * (t.k + 1))
                    width = D if t.kind == "plain" else 2 * D
                    for j in range(TILES):
                        k = t.k * TILES + j
                        weights = centred[:, k, :] if t.kind == "plain" else features[:, k, :].bitcast(f32)
                        done = nc.tensor.matmul(bank[0:width, :], weights,
                                                blocks[:, t.load["slot"], j * BLK:(j + 1) * BLK],
                                                start=first and j == 0, stop=last and j == TILES - 1)
                    done.then_inc(unsplit_used, 1)
                    return
                for c in range(CHUNKS):
                    n = t.first_chunk + c
                    pe.wait_ge(adj_lo_ready, n + 1)
                    for jj in range(CHUNK_TILES):
                        j = c * CHUNK_TILES + jj
                        if t.kind == "one":
                            weights = features[:, t.k * TILES + j, :]
                        else:
                            weights = h2_split[:, t.k % H2_BUFS, j, :]
                        cols = slice(jj * BLK, (jj + 1) * BLK)
                        nc.tensor.matmul(bank, weights, adj_hi[:, n % SPLIT_BUFS, cols],
                                         start=first and j == 0, stop=False)
                        done = nc.tensor.matmul(bank, weights, adj_lo[:, n % SPLIT_BUFS, cols],
                                                start=False, stop=last and j == TILES - 1)
                    done.then_inc(chunk_used, 1)

            def transpose_out(r):
                if r["index"] == 0:
                    pe.wait_ge(constants, 1)
                    pe.wait_ge(cleared, 5)
                    pe.wait_ge(weights_arrived, 64)
                if r["index"] >= ROW_BANKS:
                    pe.wait_ge(result_used, r["index"] - ROW_BANKS + 1)
                for q in r["sums"]:
                    pe.wait_ge(sum_copied, q.copy + 1)
                bank = row_banks[:, r["index"] % ROW_BANKS, :]
                of = {q.kind: sums_sb[:, q.copy % COPY_BUFS, :] for q in r["sums"]}
                for j in range(TILES):
                    cols = slice(j * P, (j + 1) * P)
                    if r["row"] is None:
                        [only] = of.values()
                        done = nc.tensor.matmul(bank[:, j * D:(j + 1) * D], only[:, cols], fold_w[:, :],
                                                start=True, stop=True)
                    else:
                        at = j * 2 * D
                        if "both" in of:
                            nc.tensor.matmul(bank[:, at:at + 2 * D], of["both"][:, cols], pair_w[:, :],
                                             start=True, stop=False)
                        if "plain" in of:
                            nc.tensor.matmul(bank[:, at:at + D], of["plain"][0:D, cols], fold[0:D, :],
                                             start=True, stop=False)
                        done = nc.tensor.matmul(bank[:, at:at + D], of["one"][:, cols], fold[:, :],
                                                start=len(of) == 1, stop=True)
                done.then_inc(result_ready, 1)

            for t in units + [None] * 4:
                at = t.n if t else at + 1
                if t:
                    multiply(t)
                for r in results:
                    if r["at"] + 1 == at:
                        transpose_out(r)


GROUP_OF = {k: g for g, (k0, k1) in enumerate(GROUPS) for k in range(k0, k1)}


def kernel(x, adj, L0_gnn_u, L1_gnn_W, L1_gnn_b):
    import numpy as np
    import concourse.bacc as bacc
    from concourse.bass_utils import run_bass_kernel_spmd

    def by_partition(a):
        return np.ascontiguousarray(np.asarray(a).reshape(N // P, P, D).transpose(1, 0, 2))

    blocks = np.ascontiguousarray(
        np.asarray(adj).reshape(BLOCKS, BLK, BLOCKS, TILES, P).transpose(0, 2, 4, 3, 1)
    ).reshape(BLOCKS * BLOCKS, P, TILES * BLK)
    arrays = {"x": by_partition(x), "adj": blocks, "u": by_partition(L0_gnn_u),
              "w": np.ascontiguousarray(L1_gnn_W), "b": np.ascontiguousarray(L1_gnn_b)}
    nc = bacc.Bacc("TRN2", target_bir_lowering=False, num_devices=1)
    args = [nc.dram_tensor(f"in_{name}", a.shape, mybir.dt.from_np(a.dtype), kind="ExternalInput").ap()
            for name, a in arrays.items()]
    out = nc.dram_tensor("out", (P, N // P, D), mybir.dt.float32, kind="ExternalOutput").ap()
    bass_gnn(nc, *args, out)
    r = run_bass_kernel_spmd(nc, [{f"in_{name}": a for name, a in arrays.items()}], core_ids=[0])
    return np.ascontiguousarray(r.results[0]["out"].transpose(1, 0, 2)).reshape(N, D)
```

```python
import concourse.bass as bass
from concourse import mybir
from contextlib import ExitStack


P = 128
N = 8192
D = 64
BLK = 512
BLOCKS = N // BLK
TILES = BLK // P
PARTS = 2
PART_TILES = TILES // PARTS
BAND = 2
WIDER_ROWS = 1
EVERY = 3
EARLY_SUMS = 4
SLOTS = 24
CHUNK_TILES = 1
CHUNKS = TILES // CHUNK_TILES
SPLIT_BUFS = 8
COPY_BUFS = 3
H2_BUFS = EVERY + 1
PAIR_BUFS = 2
SUM_BANKS = 6
ROW_BANKS = 2
CHAIN = 4
LEAD = 4
FIRST_WHOLE = 2
SPLIT_AHEAD = 2
GROUPS = [(0, 1), (1, 2)] + [(k, k + 2) for k in range(2, BLOCKS, 2)]
SCRATCH_SLOTS = 8
DROP = 0.1
EPS = 1e-05


class Unit:

    def __init__(self, kind, i, k):
        self.kind = kind
        self.unsplit = kind in ("plain", "both")
        self.i, self.k = i, k


class Sum:

    def __init__(self, kind, i):
        self.kind, self.i = kind, i


def stays(i, k):
    return k <= i + BAND + (i < WIDER_ROWS)


def evenly(queues, lead):
    def work(batch):
        total = [0, 0, 0]
        for t in batch:
            total[0] += 16 if t.unsplit else 8
            total[1] += 0 if t.unsplit else 11
            total[2] += 0 if t.kind == "two" and stays(t.i, t.k) else 14
        if batch[0].kind == "two":
            total[0] += 3
        return total

    whole = [sum(w) for w in zip(*(work(b) for q in queues for b in q))]
    done, merged = [0, 0, 0], []
    left = [list(q) for q in queues]
    sizes = [len(q) for q in queues]
    while any(left):
        def unevenness(n):
            after = [(a + b) / max(1, w) for a, b, w in zip(done, work(left[n][0]), whole)]
            behind = max((1 - len(q) / s for q, s in zip(left, sizes) if q), default=0) - (1 - len(left[n]) / sizes[n])
            return 20 * (max(after) - min(after)) - behind
        choice = min((n for n, q in enumerate(left) if q and (n < 2 or len(merged) >= lead or not any(left[:2]))),
                     key=unevenness)
        batch = left[choice].pop(0)
        done = [a + b for a, b in zip(done, work(batch))]
        merged.append(batch)
    return [t for batch in merged for t in batch]


def order_of_units():
    units, row_end = [], {}
    seen = set()
    behind = []
    for s in range(BLOCKS + 1):
        split, whole, last = [], [], []
        if s < BLOCKS:
            split = sorted((Unit("one", s, k) for k in range(s, BLOCKS)), key=lambda t: stays(s, t.k))
            whole = [Unit("both", s, k) for k in range(s)]
            whole, last = whole[:-1], whole[-1:]
            if s == 0:
                split = [Unit("plain" if k % 2 else "one", 0, k) for k in range(BLOCKS)]
        first, whole = whole[:FIRST_WHOLE], whole[FIRST_WHOLE:]
        again = []
        for i in range(s - BAND - 1):
            if s == BLOCKS or i % EVERY == s % EVERY:
                ks = [k for k in range(i + BAND + 1, s) if (i, k) not in seen]
                seen.update((i, k) for k in ks)
                again.append([Unit("two", i, k) for k in ks])
                for t in again[-1]:
                    t.batch = s
        kept = [[Unit("two", i, s - 1)] for i in range(max(0, s - 1 - BAND), s)] if s else []
        half = len(again) // 2
        second = kept[:1] + again[:half] + kept[1:2] + again[half:] + kept[2:]
        second = [q for q in second if q]
        if s == BLOCKS:
            second.sort(key=lambda batch: -len(batch))
            early = second[:EARLY_SUMS]
            units += [t for batch in behind for t in batch]
            units += [t for batch in early for t in batch[:-1]] + [batch[-1] for batch in early]
            units += [t for batch in second[EARLY_SUMS:] for t in batch]
            break
        now = second[:-1] if len(second) > 3 else second
        units += first
        for batch in behind:
            units += batch
        units += evenly([[[t] for t in split], [[t] for t in whole], now], max(0, LEAD - len(first)))
        units += last
        behind = second[len(now):]
        row_end[s] = max(n for n, t in enumerate(units) if t.i == s and t.kind != "two")
    return units, row_end


def plan():
    units, row_end = order_of_units()
    where = {}
    loads, sums = [], []
    last_use = {}
    for n, u in enumerate(units):
        u.n = n
        last_use[(u.i, u.k), u.kind == "two" and not stays(u.i, u.k)] = n
    for n, u in enumerate(units):
        again = u.kind == "two" and not stays(u.i, u.k)
        kept = u.kind == "two" and not again
        if kept:
            u.loads = where[u.i, u.k]
        else:
            keep = u.kind in ("one", "plain") and stays(u.i, u.k)
            last = last_use[(u.i, u.k), False] if keep else n
            u.loads = where[u.i, u.k] = [{"i": u.i, "k": u.k, "part": part, "last": last} for part in range(PARTS)]
            loads += u.loads
    free = [-1] * (SLOTS - SCRATCH_SLOTS) + [BLOCKS] * SCRATCH_SLOTS
    holder = [None] * SLOTS
    uses = [0] * SLOTS
    for load in loads:
        slot = min(range(SLOTS), key=lambda q: free[q])
        load["slot"], load["before"] = slot, holder[slot]
        uses[slot] += 1
        load["arrived"] = 16 * uses[slot]
        load["scratch"] = slot >= SLOTS - SCRATCH_SLOTS and holder[slot] is None
        last = load["last"] - (0 if units[load["last"]].unsplit else SPLIT_AHEAD)
        holder[slot], free[slot] = load, last + load["part"] / PARTS
    chunks = unsplits = 0
    for u in units:
        u.first_chunk = chunks
        if u.unsplit:
            unsplits += 1
        else:
            chunks += CHUNKS
        u.chunks, u.unsplits = chunks, unsplits
    open_sums = {}
    for u in units:
        if u.kind == "two":
            key = ("band", u.i, 0) if u.k <= u.i + BAND else ("batch", u.i, u.batch)
        else:
            key = (u.kind, u.i, 0)
        if key not in open_sums:
            open_sums[key] = Sum(*key[:2])
            open_sums[key].first = u.n
            sums.append(open_sums[key])
        u.sum = open_sums[key]
        u.sum.last = u.n
    results = []
    for s in sums:
        if s.kind in ("one", "plain", "both"):
            s.at = row_end[s.i]
        else:
            s.at = s.last
    for s, at in row_end.items():
        results.append({"at": at, "row": s, "sums": [q for q in sums if q.kind in ("one", "plain", "both") and q.i == s]})
    results += [{"at": q.at, "row": None, "i": q.i, "sums": [q]} for q in sums if q.kind not in ("one", "plain", "both")]
    results.sort(key=lambda r: r["at"])
    taken = 0
    for r in results:
        taken = r["taken"] = max(taken, r["at"] + (2 if r["row"] in (None, BLOCKS - 1) else CHAIN))
    copies = 0
    for n, r in enumerate(results):
        r["index"] = n
        for q in sorted(r["sums"], key=lambda q: q.last):
            q.copy = copies
            q.result = n
            copies += 1
    bank_free = [(-1, None)] * SUM_BANKS
    for q in sorted(sums, key=lambda q: q.first):
        bank = min(range(SUM_BANKS), key=lambda b: bank_free[b][0])
        q.bank, q.before = bank, bank_free[bank][1]
        assert bank_free[bank][0] < q.first, "more open sums than banks"
        bank_free[bank] = (q.at, q)
    return units, loads, results


def bass_gnn(nc, x, adj, u, w, b, out):
    f32, f32r = mybir.dt.float32, mybir.dt.float32r
    ALU, ACT, AX = mybir.AluOpType, mybir.ActivationFunctionType, mybir.AxisListType

    units, loads, results = plan()
    last_result_of = {}
    for r in results:
        last_result_of[r["row"] if r["row"] is not None else r["i"]] = r["index"]
    copied = {q.copy: q for r in results for q in r["sums"]}
    last_h2_use = {t.k: t for t in units if t.kind == "two"}

    with ExitStack() as ctx:
        def sb(name, shape, dt=f32):
            return ctx.enter_context(nc.sbuf_tensor(name, shape, dt))

        def sem(name):
            return ctx.enter_context(nc.semaphore(name))

        blocks = sb("blocks", [P, SLOTS, PART_TILES * BLK])
        adj_hi = sb("adj_hi", [P, SPLIT_BUFS, CHUNK_TILES * BLK], f32r)
        adj_lo = sb("adj_lo", [P, SPLIT_BUFS, CHUNK_TILES * BLK], f32r)
        features = sb("features", [P, N // P, 2 * D], f32r)
        pair = sb("pair", [P, PAIR_BUFS, TILES, 2 * D])
        h2_split = sb("h2_split", [P, H2_BUFS, TILES, 2 * D], f32r)
        rows = sb("rows", [P, N // P, D])
        sums_sb = sb("sums_sb", [P, COPY_BUFS, BLK])
        fold = sb("fold", [P, D])
        fold_w = sb("fold_w", [P, D])
        pair_w = sb("pair_w", [P, 2 * D])
        bias = sb("bias", [P, D])
        eps = sb("eps", [P, 1])
        total = sb("total", [P, N // P])
        square = sb("square", [P, N // P])
        dev = sb("dev", [P, N // P])
        total2 = sb("total2", [P, TILES])
        square2 = sb("square2", [P, TILES])
        dev2 = sb("dev2", [P, TILES])
        centred2 = sb("centred2", [P, TILES, D])
        squares2 = sb("squares2", [P, TILES, D])
        scratch = blocks[:, SLOTS - SCRATCH_SLOTS:SLOTS, :].rearrange("p s n -> p (s n)")
        u_sb = scratch[:, 0:N // P * D].rearrange("p (t d) -> p t d", d=D)
        centred = scratch[:, N // P * D:2 * N // P * D].rearrange("p (t d) -> p t d", d=D)

        x_squares = sums_sb[:, :, :].rearrange("p b (t d) -> p b t d", d=D)

        banks = ctx.enter_context(nc.psum_tensor("banks", [P, SUM_BANKS, BLK], f32))
        row_banks = ctx.enter_context(nc.psum_tensor("row_banks", [P, ROW_BANKS, BLK], f32))

        block_arrived = [sem(f"block_arrived{n}") for n in range(SLOTS)]
        x_arrived = [sem(f"x_arrived{n}") for n in range(len(GROUPS))]
        u_arrived = [sem(f"u_arrived{n}") for n in range(len(GROUPS))]
        weights_arrived = sem("weights_arrived")
        cleared = sem("cleared")
        constants = sem("constants")
        x_step = sem("x_step")
        warm = sem("warm")
        x_centred = sem("x_centred")
        x_squared = sem("x_squared")
        x_summed = sem("x_summed")
        x_dev = sem("x_dev")
        x_scale = sem("x_scale")
        keep_ready = sem("keep_ready")
        keep_scaled = sem("keep_scaled")
        xd_ready = sem("xd_ready")
        xd_hi_ready = sem("xd_hi_ready")
        xd_split_ready = sem("xd_split_ready")
        adj_hi_ready = sem("adj_hi_ready")
        adj_lo_ready = sem("adj_lo_ready")
        chunk_used = sem("chunk_used")
        unsplit_used = sem("unsplit_used")
        sum_copied = sem("sum_copied")
        result_ready = sem("result_ready")
        result_used = sem("result_used")
        h2_step = sem("h2_step")
        h2_summed = sem("h2_summed")
        h2_dev = sem("h2_dev")
        h2_ready = sem("h2_ready")
        pair_ready = sem("pair_ready")
        pair_arrived = sem("pair_arrived")
        stored = sem("stored")
        block = ctx.enter_context(nc.Block())

        def wait_sum_complete(eng, q):
            t = units[q.last]
            if t.unsplit:
                eng.wait_ge(unsplit_used, PARTS * t.unsplits)
            else:
                eng.wait_ge(chunk_used, t.chunks)

        def arrived(eng, load):
            eng.wait_ge(block_arrived[load["slot"]], load["arrived"])

        def chunk_of(t, c):
            load = t.loads[c * PARTS // CHUNKS]
            at = c * CHUNK_TILES % PART_TILES * BLK
            return load, blocks[:, load["slot"], at:at + CHUNK_TILES * BLK]

        def tiles_of(k):
            return slice(k * TILES, (k + 1) * TILES)

        @block.sync
        def _(sp):
            t = slice(0, GROUPS[0][1] * TILES)
            sp.dma_start(rows[:, t, :], x[:, t, :]).then_inc(x_arrived[0], 16)
            sp.dma_start(u_sb[:, t, :], u[:, t, :]).then_inc(u_arrived[0], 16)
            for load in loads:
                before = load["before"]
                if before is not None:
                    t = units[before["last"]]
                    if t.unsplit:
                        sp.wait_ge(unsplit_used, PARTS * (t.unsplits - 1) + before["part"] + 1)
                    else:
                        sp.wait_ge(adj_lo_ready, t.first_chunk + (before["part"] + 1) * CHUNKS // PARTS)
                elif load["scratch"]:
                    sp.wait_ge(xd_split_ready, len(GROUPS))
                    sp.wait_ge(unsplit_used, PARTS * units[BLOCKS - 1].unsplits)
                sp.dma_start(blocks[:, load["slot"], :],
                             adj[(load["i"] * BLOCKS + load["k"]) * PARTS + load["part"], :, :])\
                    .then_inc(block_arrived[load["slot"]], 16)
            order = sorted(range(BLOCKS), key=lambda i: last_result_of[i])
            for i in order:
                sp.wait_ge(result_used, last_result_of[i] + 1)
                sp.dma_start(out[:, tiles_of(i), :], rows[:, tiles_of(i), :]).then_inc(stored, 16)
            sp.wait_ge(stored, 16 * BLOCKS)

        @block.gpsimd
        def _(pool):
            nc.gpsimd.memset(eps[:, :], EPS).then_inc(cleared, 1)
            nc.gpsimd.memset(fold[:, :], 0.0).then_inc(cleared, 1)
            nc.gpsimd.memset(pair_w[:, :], 0.0).then_inc(cleared, 1)
            pool.wait_ge(cleared, 3)
            nc.gpsimd.affine_select(out=fold[:, :], in_=fold[:, :], compare_op=ALU.not_equal, fill=1.0,
                                    base=0, pattern=[[-1, D]], channel_multiplier=1).then_inc(cleared, 1)
            nc.gpsimd.affine_select(out=pair_w[:, 0:D], in_=pair_w[:, 0:D], compare_op=ALU.not_equal, fill=1.0,
                                    base=0, pattern=[[-1, D]], channel_multiplier=1).then_inc(cleared, 1)
            pool.wait_ge(cleared, 5)
            nc.gpsimd.affine_select(out=fold[:, :], in_=fold[:, :], compare_op=ALU.not_equal, fill=1.0,
                                    base=-D, pattern=[[-1, D]], channel_multiplier=1).then_inc(constants, 1)
            pool.dma_start(pair_w[D:P, D:2 * D], w).then_inc(weights_arrived, 16)
            pool.dma_start(fold_w[0:D, :], w).then_inc(weights_arrived, 16)
            pool.dma_start(fold_w[D:P, :], w).then_inc(weights_arrived, 16)
            pool.dma_start(bias[:, :], b.rearrange("(a n) -> a n", a=1).to_broadcast([P, D]))\
                .then_inc(weights_arrived, 16)
            for g, (k0, k1) in enumerate(GROUPS):
                t = slice(k0 * TILES, k1 * TILES)
                pool.wait_ge(u_arrived[g], 16)
                nc.gpsimd.tensor_scalar(u_sb[:, t, :], u_sb[:, t, :], DROP, 1.0 / (1.0 - DROP),
                                        ALU.is_ge, ALU.mult).then_inc(keep_ready, 1)
                pool.wait_ge(keep_ready, g + 1)
                pool.wait_ge(x_scale, g + 1)
                shape = [P, (k1 - k0) * TILES, D]
                nc.gpsimd.tensor_tensor(u_sb[:, t, :], u_sb[:, t, :], square[:, t].unsqueeze(2).to_broadcast(shape),
                                        ALU.mult).then_inc(keep_scaled, 1)

        @block.scalar
        def _(act):
            for g, (k0, k1) in list(enumerate(GROUPS))[1:]:
                t = slice(k0 * TILES, k1 * TILES)
                act.dma_start(rows[:, t, :], x[:, t, :]).then_inc(x_arrived[g], 16)
                act.dma_start(u_sb[:, t, :], u[:, t, :]).then_inc(u_arrived[g], 16)
            act.wait_ge(cleared, 1)

            def square_x(g):
                t = slice(GROUPS[g][0] * TILES, GROUPS[g][1] * TILES)
                act.wait_ge(x_centred, g + 1)
                n = t.stop - t.start
                nc.scalar.activation(x_squares[:, g % COPY_BUFS, 0:n, :], centred[:, t, :], ACT.Square)\
                    .then_inc(x_squared, 1)

            def deviation_x(g):
                t = slice(GROUPS[g][0] * TILES, GROUPS[g][1] * TILES)
                act.wait_ge(x_summed, g + 1)
                nc.scalar.activation(dev[:, t], square[:, t], ACT.Sqrt, bias=eps[:, 0:1], scale=1.0 / D)\
                    .then_inc(x_dev, 1)

            def xd_hi(g):
                t = slice(GROUPS[g][0] * TILES, GROUPS[g][1] * TILES)
                act.wait_ge(xd_ready, g + 1)
                nc.scalar.activation(features[:, t, 0:D], centred[:, t, :], ACT.Copy).then_inc(xd_hi_ready, 1)

            def split(t, chunks=range(CHUNKS)):
                for c in chunks:
                    n = t.first_chunk + c
                    load, chunk = chunk_of(t, c)
                    arrived(act, load)
                    if n >= SPLIT_BUFS:
                        act.wait_ge(chunk_used, n - SPLIT_BUFS + 1)
                    nc.scalar.activation(adj_hi[:, n % SPLIT_BUFS, :], chunk, ACT.Copy).then_inc(adj_hi_ready, 1)

            def copy_out(r):
                for q in sorted(r["sums"], key=lambda q: q.copy):
                    wait_sum_complete(act, q)
                    if q.copy >= COPY_BUFS:
                        act.wait_ge(result_ready, copied[q.copy - COPY_BUFS].result + 1)
                    height = D if q.kind == "plain" else P
                    nc.scalar.activation(sums_sb[0:height, q.copy % COPY_BUFS, :], banks[0:height, q.bank, :], ACT.Copy)\
                        .then_inc(sum_copied, 1)

            def place_pair(s):
                act.wait_ge(h2_ready, s + 1)
                act.wait_ge(pair_ready, s + 1)
                act.dma_start(features[:, tiles_of(s), :].bitcast(f32), pair[:, s % PAIR_BUFS, :, :])\
                    .then_inc(pair_arrived, 16)

            def deviation(s):
                act.wait_ge(h2_summed, s + 1)
                nc.scalar.activation(dev2[:, :], square2[:, :], ACT.Sqrt, bias=eps[:, 0:1], scale=1.0 / D)\
                    .then_inc(h2_dev, 1)

            nc.scalar.activation(dev[:, 0:1], eps[:, 0:1], ACT.Sqrt).then_inc(warm, 1)
            act.wait_ge(warm, 1)
            for g in range(len(GROUPS) + 1):
                ahead = [t for t in units[:BLOCKS] if g and GROUP_OF[t.k] == g - 1 and not t.unsplit]
                for t in ahead:
                    split(t, range(CHUNKS // 2))
                if g < len(GROUPS):
                    square_x(g)
                for t in ahead:
                    split(t, range(CHUNKS // 2, CHUNKS))
                if g < len(GROUPS):
                    deviation_x(g)
                if g:
                    xd_hi(g - 1)

            for t in units[BLOCKS:] + [None] * 4:
                at = t.n if t else at + 1
                if t and not t.unsplit:
                    split(t)
                for r in results:
                    if r["at"] + 1 == at:
                        copy_out(r)
                for r in results:
                    if r["taken"] == at and r["row"] is not None:
                        deviation(r["row"])
                    if r["taken"] + 2 == at and r["row"] is not None and r["row"] < BLOCKS - 1:
                        place_pair(r["row"])

        @block.vector
        def _(dve):
            steps = [0]

            def link(semaphore, instruction):
                steps[0] += 1
                instruction.then_inc(semaphore, 1)
                dve.wait_ge(semaphore, steps[0])

            def tiles_of_group(g):
                k0, k1 = GROUPS[g]
                return slice(k0 * TILES, k1 * TILES), [P, (k1 - k0) * TILES, D]

            def centre_x(g):
                t, shape = tiles_of_group(g)
                dve.wait_ge(x_arrived[g], 16)
                link(x_step, nc.vector.tensor_reduce(total[:, t], rows[:, t, :], AX.X, ALU.add))
                link(x_step, nc.vector.tensor_scalar(total[:, t], total[:, t], -1.0 / D, None, ALU.mult))
                nc.vector.tensor_tensor(centred[:, t, :], rows[:, t, :], total[:, t].unsqueeze(2).to_broadcast(shape),
                                        ALU.add).then_inc(x_centred, 1)

            def sum_squares_x(g):
                t, _ = tiles_of_group(g)
                dve.wait_ge(x_squared, g + 1)
                n = t.stop - t.start
                nc.vector.tensor_reduce(square[:, t], x_squares[:, g % COPY_BUFS, 0:n, :], AX.X, ALU.add)\
                    .then_inc(x_summed, 1)

            def scale_x(g):
                t, _ = tiles_of_group(g)
                dve.wait_ge(x_dev, g + 1)
                nc.vector.reciprocal(square[:, t], dev[:, t]).then_inc(x_scale, 1)

            def drop_x(g):
                t, _ = tiles_of_group(g)
                dve.wait_ge(keep_scaled, g + 1)
                nc.vector.scalar_tensor_tensor(out=centred[:, t, :], in0=centred[:, t, :], scalar=0.0,
                                               in1=u_sb[:, t, :], op0=ALU.max, op1=ALU.mult).then_inc(xd_ready, 1)

            def xd_lo(g):
                t, _ = tiles_of_group(g)
                dve.wait_ge(xd_hi_ready, g + 1)
                nc.vector.tensor_tensor(features[:, t, D:2 * D], centred[:, t, :], features[:, t, 0:D].bitcast(f32),
                                        ALU.subtract).then_inc(xd_split_ready, 1)

            def split(t, chunks=range(CHUNKS)):
                for c in chunks:
                    n = t.first_chunk + c
                    dve.wait_ge(adj_hi_ready, n + 1)
                    _, chunk = chunk_of(t, c)
                    nc.vector.tensor_tensor(adj_lo[:, n % SPLIT_BUFS, :], chunk,
                                            adj_hi[:, n % SPLIT_BUFS, :].bitcast(f32), ALU.subtract)\
                        .then_inc(adj_lo_ready, 1)

            h2_steps = [0]

            def link2(instruction):
                h2_steps[0] += 1
                instruction.then_inc(h2_step, 1)
                dve.wait_ge(h2_step, h2_steps[0])

            def row_of_layer_1(r):
                s = r["row"]
                shape = [P, TILES, D]
                mine = rows[:, tiles_of(s), :]
                bank = row_banks[:, r["index"] % ROW_BANKS, :].rearrange("p (t e) -> p t e", e=2 * D)
                dve.wait_ge(result_ready, r["index"] + 1)
                link2(nc.vector.tensor_tensor(mine, mine, bank[:, :, 0:D], ALU.add))
                link2(nc.vector.tensor_reduce(total2[:, :], mine, AX.X, ALU.add))
                link2(nc.vector.tensor_scalar(total2[:, :], total2[:, :], -1.0 / D, None, ALU.mult))
                link2(nc.vector.tensor_tensor(centred2[:, :, :], mine, total2[:, :].unsqueeze(2).to_broadcast(shape),
                                              ALU.add))
                link2(nc.vector.tensor_tensor(squares2[:, :, :], centred2[:, :, :], centred2[:, :, :], ALU.mult))
                nc.vector.tensor_reduce(square2[:, :], squares2[:, :, :], AX.X, ALU.add).then_inc(h2_summed, 1)
                if s > 0:
                    link2(nc.vector.tensor_tensor(mine, mine, bank[:, :, D:2 * D], ALU.add))
                dve.wait_ge(weights_arrived, 64)
                nc.vector.tensor_tensor(mine, mine, bias[:, :].unsqueeze(1).to_broadcast(shape), ALU.add)\
                    .then_inc(result_used, 1)
                dve.wait_ge(h2_dev, s + 1)
                link2(nc.vector.reciprocal(square2[:, :], dev2[:, :]))
                h2 = pair[:, s % PAIR_BUFS, :, D:2 * D]
                split_h2 = h2_split[:, s % H2_BUFS, :, :]
                if s >= PAIR_BUFS:
                    dve.wait_ge(pair_arrived, 16 * (s - PAIR_BUFS + 1))
                link2(nc.vector.scalar_tensor_tensor(
                    out=h2, in0=centred2[:, :, :], scalar=0.0,
                    in1=square2[:, :].unsqueeze(2).to_broadcast(shape), op0=ALU.max, op1=ALU.mult))
                if s >= H2_BUFS:
                    dve.wait_ge(chunk_used, last_h2_use[s - H2_BUFS].chunks)
                link2(nc.vector.tensor_copy(split_h2[:, :, 0:D], h2))
                nc.vector.tensor_tensor(split_h2[:, :, D:2 * D], h2, split_h2[:, :, 0:D].bitcast(f32),
                                        ALU.subtract).then_inc(h2_ready, 1)
                if s < BLOCKS - 1:
                    mine = features[:, tiles_of(s), :].bitcast(f32)
                    nc.vector.tensor_tensor(pair[:, s % PAIR_BUFS, :, 0:D], mine[:, :, 0:D], mine[:, :, D:2 * D],
                                            ALU.add).then_inc(pair_ready, 1)

            def part_of_layer_2(r):
                mine = rows[:, tiles_of(r["i"]), :]
                bank = row_banks[:, r["index"] % ROW_BANKS, 0:TILES * D].rearrange("p (t d) -> p t d", d=D)
                dve.wait_ge(result_ready, r["index"] + 1)
                if r["index"] >= 1:
                    dve.wait_ge(result_used, r["index"])
                nc.vector.tensor_tensor(mine, mine, bank, ALU.add).then_inc(result_used, 1)

            for g in range(len(GROUPS) + 1):
                ahead = [t for t in units[:BLOCKS] if g and GROUP_OF[t.k] == g - 1 and not t.unsplit]
                if g < len(GROUPS):
                    centre_x(g)
                if g:
                    scale_x(g - 1)
                for t in ahead:
                    split(t, range(CHUNKS // 2))
                if g < len(GROUPS):
                    sum_squares_x(g)
                if g:
                    drop_x(g - 1)
                for t in ahead:
                    split(t, range(CHUNKS // 2, CHUNKS))
                if g:
                    xd_lo(g - 1)

            for t in units[BLOCKS:] + [None] * 4:
                at = t.n if t else at + 1
                if t and not t.unsplit:
                    split(t)
                for r in results:
                    if r["taken"] == at:
                        if r["row"] is not None:
                            row_of_layer_1(r)
                        else:
                            part_of_layer_2(r)

        @block.tensor
        def _(pe):
            def multiply(t):
                q = t.sum
                bank = banks[:, q.bank, :]
                first, last = t.n == q.first, t.n == q.last
                if first and q.before is not None:
                    pe.wait_ge(sum_copied, q.before.copy + 1)
                if t.kind == "one" and t.i == 0:
                    pe.wait_ge(xd_split_ready, GROUP_OF[t.k] + 1)
                if t.kind == "plain":
                    pe.wait_ge(xd_ready, GROUP_OF[t.k] + 1)
                if t.kind == "two":
                    pe.wait_ge(h2_ready, t.k + 1)
                if t.unsplit:
                    if t.kind == "both":
                        pe.wait_ge(pair_arrived, 16 * (t.k + 1))
                    width = D if t.kind == "plain" else 2 * D
                    for j in range(TILES):
                        load, at = t.loads[j // PART_TILES], j % PART_TILES * BLK
                        if j % PART_TILES == 0:
                            arrived(pe, load)
                        k = t.k * TILES + j
                        weights = centred[:, k, :] if t.kind == "plain" else features[:, k, :].bitcast(f32)
                        done = nc.tensor.matmul(bank[0:width, :], weights,
                                                blocks[:, load["slot"], at:at + BLK],
                                                start=first and j == 0, stop=last and j == TILES - 1)
                        if j % PART_TILES == PART_TILES - 1:
                            done.then_inc(unsplit_used, 1)
                    return
                for c in range(CHUNKS):
                    n = t.first_chunk + c
                    pe.wait_ge(adj_lo_ready, n + 1)
                    for jj in range(CHUNK_TILES):
                        j = c * CHUNK_TILES + jj
                        if t.kind == "one":
                            weights = features[:, t.k * TILES + j, :]
                        else:
                            weights = h2_split[:, t.k % H2_BUFS, j, :]
                        cols = slice(jj * BLK, (jj + 1) * BLK)
                        nc.tensor.matmul(bank, weights, adj_hi[:, n % SPLIT_BUFS, cols],
                                         start=first and j == 0, stop=False)
                        done = nc.tensor.matmul(bank, weights, adj_lo[:, n % SPLIT_BUFS, cols],
                                                start=False, stop=last and j == TILES - 1)
                    done.then_inc(chunk_used, 1)

            def transpose_out(r):
                if r["index"] == 0:
                    pe.wait_ge(constants, 1)
                    pe.wait_ge(cleared, 5)
                    pe.wait_ge(weights_arrived, 64)
                if r["index"] >= ROW_BANKS:
                    pe.wait_ge(result_used, r["index"] - ROW_BANKS + 1)
                for q in r["sums"]:
                    pe.wait_ge(sum_copied, q.copy + 1)
                bank = row_banks[:, r["index"] % ROW_BANKS, :]
                of = {q.kind: sums_sb[:, q.copy % COPY_BUFS, :] for q in r["sums"]}
                for j in range(TILES):
                    cols = slice(j * P, (j + 1) * P)
                    if r["row"] is None:
                        [only] = of.values()
                        done = nc.tensor.matmul(bank[:, j * D:(j + 1) * D], only[:, cols], fold_w[:, :],
                                                start=True, stop=True)
                    else:
                        at = j * 2 * D
                        if "both" in of:
                            nc.tensor.matmul(bank[:, at:at + 2 * D], of["both"][:, cols], pair_w[:, :],
                                             start=True, stop=False)
                        if "plain" in of:
                            nc.tensor.matmul(bank[:, at:at + D], of["plain"][0:D, cols], fold[0:D, :],
                                             start=True, stop=False)
                        done = nc.tensor.matmul(bank[:, at:at + D], of["one"][:, cols], fold[:, :],
                                                start=len(of) == 1, stop=True)
                done.then_inc(result_ready, 1)

            for t in units + [None] * 4:
                at = t.n if t else at + 1
                if t:
                    multiply(t)
                for r in results:
                    if r["at"] + 1 == at:
                        transpose_out(r)


GROUP_OF = {k: g for g, (k0, k1) in enumerate(GROUPS) for k in range(k0, k1)}


def kernel(x, adj, L0_gnn_u, L1_gnn_W, L1_gnn_b):
    import numpy as np
    import concourse.bacc as bacc
    from concourse.bass_utils import run_bass_kernel_spmd

    def by_partition(a):
        return np.ascontiguousarray(np.asarray(a).reshape(N // P, P, D).transpose(1, 0, 2))

    blocks = np.ascontiguousarray(
        np.asarray(adj).reshape(BLOCKS, BLK, BLOCKS, PARTS, PART_TILES, P).transpose(0, 2, 3, 5, 4, 1)
    ).reshape(BLOCKS * BLOCKS * PARTS, P, PART_TILES * BLK)
    arrays = {"x": by_partition(x), "adj": blocks, "u": by_partition(L0_gnn_u),
              "w": np.ascontiguousarray(L1_gnn_W), "b": np.ascontiguousarray(L1_gnn_b)}
    nc = bacc.Bacc("TRN2", target_bir_lowering=False, num_devices=1)
    args = [nc.dram_tensor(f"in_{name}", a.shape, mybir.dt.from_np(a.dtype), kind="ExternalInput").ap()
            for name, a in arrays.items()]
    out = nc.dram_tensor("out", (P, N // P, D), mybir.dt.float32, kind="ExternalOutput").ap()
    bass_gnn(nc, *args, out)
    r = run_bass_kernel_spmd(nc, [{f"in_{name}": a for name, a in arrays.items()}], core_ids=[0])
    return np.ascontiguousarray(r.results[0]["out"].transpose(1, 0, 2)).reshape(N, D)
```
